# Optimizing a Trainium2 kernel written in Bass

```python
import numpy as np
import jax
import jax.numpy as jnp

def _softmax(x, axis=-1):
    return jax.nn.softmax(x, axis=axis)

def _gelu(x):
    return jax.nn.gelu(x, approximate=True)

def _silu(x):
    return jax.nn.silu(x)

def _sigmoid(x):
    return jax.nn.sigmoid(x)

def _layernorm(x, axis=-1, eps=1e-05):
    m = jnp.mean(x, axis=axis, keepdims=True)
    v = jnp.var(x, axis=axis, keepdims=True)
    return (x - m) / jnp.sqrt(v + eps)

def _scatter_add(tgt, idx, src, axis=0):
    return tgt.at[idx].add(src)

def _segment_sum(src, seg, n):
    return jax.ops.segment_sum(src, seg, n)
kernel_name = 'mk_conv_seq_d1_conv_nchw512_r4_563306'

def setup_inputs(seed: int=0):
    np.random.seed(seed)
    _w = jnp.asarray

    def _rec_inputs():
        import jax
        import jax.numpy as jnp
        _gk = jax.random.key(seed)
        x = -0.000125 + 0.9999 * jax.random.normal(jax.random.fold_in(_gk, 1), (16, 128, 16, 16), jnp.float32)
        return x
    x = _rec_inputs()

    def _L0_conv_setup():
        import jax, jax.numpy as jnp
        import numpy as np
        B, C, H, W, HEADS = (16, 128, 16, 16, 8)
        EPS = 1e-05
        key = jax.random.key(seed)
        ks = jax.random.split(key, 5)
        s = C ** (-0.5)
        return {'x': jax.random.normal(ks[0], (B, C, H, W), dtype=jnp.float32), 'Wq': jax.random.normal(ks[1], (C, C), dtype=jnp.float32) * s, 'Wk': jax.random.normal(ks[2], (C, C), dtype=jnp.float32) * s, 'Wv': jax.random.normal(ks[3], (C, C), dtype=jnp.float32) * s, 'Wo': jax.random.normal(ks[4], (C, C), dtype=jnp.float32) * s, 'gamma': jnp.ones((C,), dtype=jnp.float32), 'beta': jnp.zeros((C,), dtype=jnp.float32)}
    _L0_conv_all = _L0_conv_setup()
    _L0_conv_in = {k: v for k, v in _L0_conv_all.items() if k in ('Wq', 'Wk', 'Wv', 'Wo', 'gamma', 'beta')}
    del _L0_conv_all
    return {'x': x, 'L0_conv_Wq': _L0_conv_in['Wq'], 'L0_conv_Wk': _L0_conv_in['Wk'], 'L0_conv_Wv': _L0_conv_in['Wv'], 'L0_conv_Wo': _L0_conv_in['Wo'], 'L0_conv_gamma': _L0_conv_in['gamma'], 'L0_conv_beta': _L0_conv_in['beta']}

def reference(x, L0_conv_Wq, L0_conv_Wk, L0_conv_Wv, L0_conv_Wo, L0_conv_gamma, L0_conv_beta):
    import jax
    import jax.numpy as jnp

    def _L0_conv_ref(x, Wq, Wk, Wv, Wo, gamma, beta):
        import jax, jax.numpy as jnp
        import numpy as np
        B, C, H, W, HEADS = (16, 128, 16, 16, 8)
        EPS = 1e-05
        Bb, Cc, Hh, Ww = x.shape
        d = Cc // HEADS
        n = Hh * Ww

        def proj(Wt):
            return jnp.einsum('oc,bchw->bohw', Wt, x).reshape(Bb, HEADS, d, n)
        q = proj(Wq)
        k = proj(Wk)
        v = proj(Wv)
        k = jax.nn.softmax(k, axis=-2)
        context = jnp.einsum('bhdn,bhen->bhde', k, v)
        out = jnp.einsum('bhdn,bhde->bhen', q, context)
        out = out.reshape(Bb, Cc, Hh, Ww)
        out = jnp.einsum('oc,bchw->bohw', Wo, out)
        y = out + x
        mean = jnp.mean(y, axis=(0, 2, 3), keepdims=True)
        var = jnp.var(y, axis=(0, 2, 3), keepdims=True)
        yn = (y - mean) * jax.lax.rsqrt(var + EPS)
        return yn * gamma[None, :, None, None] + beta[None, :, None, None]

    def _gn(v, G=32, eps=1e-05):
        B_, C_, H_, W_ = v.shape
        g = v.reshape(B_, G, C_ // G, H_, W_)
        m = jnp.mean(g, axis=(2, 3, 4), keepdims=True)
        s = jnp.var(g, axis=(2, 3, 4), keepdims=True)
        return ((g - m) / jnp.sqrt(s + eps)).reshape(v.shape)

    def _ln_c(v, eps=1e-06):
        m = jnp.mean(v, axis=1, keepdims=True)
        s = jnp.var(v, axis=1, keepdims=True)
        return (v - m) / jnp.sqrt(s + eps)

    def _ln_t(v, eps=1e-05):
        m = jnp.mean(v, axis=-1, keepdims=True)
        s = jnp.var(v, axis=-1, keepdims=True)
        return (v - m) / jnp.sqrt(s + eps)

    def _to_tokens(v):
        B_, C_, H_, W_ = v.shape
        return v.reshape(B_, C_, H_ * W_).transpose(0, 2, 1)

    def _from_tokens(t, like):
        B_, C_, H_, W_ = like.shape
        return t.transpose(0, 2, 1).reshape(B_, C_, H_, W_)
    x = _L0_conv_ref(x, L0_conv_Wq, L0_conv_Wk, L0_conv_Wv, L0_conv_Wo, L0_conv_gamma, L0_conv_beta)
    return x

_drawn_inputs = setup_inputs


def setup_inputs(seed=0):
    import zlib

    import numpy as np

    out = dict(_drawn_inputs(seed))
    spreads = {'L0_conv_gamma': (1.0, 0.2), 'L0_conv_beta': (0.0, 0.1)}
    factors = {}
    for name, (base, spread) in spreads.items():
        noise = np.random.default_rng([zlib.crc32(name.encode()), seed]).standard_normal(out[name].shape)
        drawn = base * np.exp(spread * noise) if base else spread * noise
        out[name] = jnp.asarray(drawn.astype(out[name].dtype))
    for name, factor in factors.items():
        out[name] = (out[name] * factor).astype(out[name].dtype)
    return out
```

```python
from contextlib import ExitStack

import concourse.bass as bass
from concourse import mybir

ALU = mybir.AluOpType
ACT = mybir.ActivationFunctionType
AX = mybir.AxisListType
F32 = mybir.dt.float32
F32R = mybir.dt.float32r
BF16 = mybir.dt.bfloat16

B = 16
C = 128
N = 256
HEADS = 8
D = C // HEADS
CH = N // 128
PAIRS = B // 2
PN = 2 * N
EPS = 1e-5


def attention_batchnorm(nc: bass.Bass, x, w, affine, out):
    with ExitStack() as ctx:
        def sb(name, shape, dt=F32):
            return ctx.enter_context(nc.sbuf_tensor(name, shape, dt))

        def ps(name, shape, dt=F32):
            return ctx.enter_context(nc.psum_tensor(name, shape, dt))

        def sem(name):
            return ctx.enter_context(nc.semaphore(name))

        w_sb = sb("w_sb", [C, 4 * C])
        wkv = w_sb[:, 0:2 * C]
        wq = w_sb[:, 2 * C:3 * C]
        woT = w_sb[:, 3 * C:4 * C]
        wkv_hi = sb("wkv_hi", [C, 2 * C], F32R)
        wkv_lo = sb("wkv_lo", [C, 2 * C], F32R)
        head_mask = sb("head_mask", [C, C])
        identity = sb("identity", [C, 2, C], BF16)
        gamma_beta = sb("gamma_beta", [C, 2])
        x_sb = sb("x_sb", [C, PAIRS, PN])
        y_sb = sb("y_sb", [C, PAIRS, PN])
        x_hi = sb("x_hi", [C, PAIRS, PN], F32R)
        x_lo = sb("x_lo", [C, PAIRS, PN], F32R)
        k_max = sb("k_max", [128, PAIRS, 2 * CH * HEADS])
        probs = sb("probs", [128, PAIRS, 2 * CH, C])
        k_sum = sb("k_sum", [128, PAIRS, 2 * CH * HEADS])
        k_inv = sb("k_inv", [128, PAIRS, 2 * CH * HEADS])
        v_sb = sb("v_sb", [128, PAIRS, 2 * CH, C])
        ct_sb = sb("ct_sb", [C, PAIRS, 2, C])
        u_sb = sb("u_sb", [C, PAIRS, 2 * C])
        a_hi = sb("a_hi", [C, PAIRS, 2 * C], F32R)
        a_lo = sb("a_lo", [C, PAIRS, 2 * C], F32R)
        stats = sb("stats", [C, PAIRS * 6])
        mean_var = sb("mean_var", [C, 2])
        var_eps = sb("var_eps", [C, 1])
        std = sb("std", [C, 1])
        rstd = sb("rstd", [C, 1])
        scale = sb("scale", [C, 1])
        mean_scale = sb("mean_scale", [C, 1])
        shift = sb("shift", [C, 1])

        kv_ps = ps("kv_ps", [128, 2, 2 * CH, 2 * C])
        ct_ps = ps("ct_ps", [C, 512])
        u_ps = ps("u_ps", [C, 512])
        a_ps = ps("a_ps", [C, 512])
        y_ps = ps("y_ps", [C, PN])

        w_landed = sem("w_landed")
        affine_landed = sem("affine_landed")
        x_landed = [sem(f"x_landed{i}") for i in range(4)]
        mask_zeroed = sem("mask_zeroed")
        consts_ready = sem("consts_ready")
        w_hi_ready = sem("w_hi_ready")
        w_lo_ready = sem("w_lo_ready")
        x_hi_ready = sem("x_hi_ready")
        x_lo_ready = sem("x_lo_ready")
        kv_ready = sem("kv_ready")
        max_ready = sem("max_ready")
        shift_ready = sem("shift_ready")
        exp_ready = sem("exp_ready")
        sum_ready = sem("sum_ready")
        inv_ready = sem("inv_ready")
        probs_ready = sem("probs_ready")
        v_ready = sem("v_ready")
        ct_ready = sem("ct_ready")
        ct_masked = sem("ct_masked")
        u_ready = sem("u_ready")
        u_copied = sem("u_copied")
        a_ready = sem("a_ready")
        a_hi_ready = sem("a_hi_ready")
        a_lo_ready = sem("a_lo_ready")
        y_ready = sem("y_ready")
        y_copied = sem("y_copied")
        y_counted = sem("y_counted")
        final_step = sem("final_step")
        std_ready = sem("std_ready")
        affine_ready = sem("affine_ready")
        out_by_vector = sem("out_by_vector")
        out_by_scalar = sem("out_by_scalar")
        stored = sem("stored")

        PIECES = [(0, 1), (1, 2), (2, 4), (4, 8)]
        x_view = x_sb[:, :, :].rearrange("c p (b n) -> c (p b) n", n=N)
        y_view = y_sb[:, :, :].rearrange("c p (b n) -> c (p b) n", n=N)
        LAST_OF_VECTOR = {0: 1, 1: 2, 3: 3, 4: 4, 6: 5}
        LAST_OF_SCALAR = {2: 1, 5: 2, 7: 3}

        def run_slots(*stages):
            for t in range(-1, PAIRS + 5):
                for stage, lag in stages:
                    if 0 <= t - lag < PAIRS:
                        stage(t - lag)

        block = ctx.enter_context(nc.Block())

        @block.sync
        def _(sp):
            sp.dma_start(x_view[:, 0:2, :], x[0:2].rearrange("b c n -> c b n")).then_inc(x_landed[0], 16)
            sp.dma_start(w_sb[:, :], w).then_inc(w_landed, 16)
            for i, (lo, hi) in enumerate(PIECES[1:], 1):
                sp.dma_start(x_view[:, 2 * lo:2 * hi, :],
                             x[2 * lo:2 * hi].rearrange("b c n -> c b n")).then_inc(x_landed[i], 16)
            sp.dma_start(gamma_beta[:, :], affine).then_inc(affine_landed, 16)
            for p in range(PAIRS):
                if p in LAST_OF_VECTOR:
                    sp.wait_ge(out_by_vector, LAST_OF_VECTOR[p])
                else:
                    sp.wait_ge(out_by_scalar, LAST_OF_SCALAR[p])
                sp.dma_start(out[2 * p:2 * p + 2].rearrange("b c n -> c b n"),
                             y_view[:, 2 * p:2 * p + 2, :]).then_inc(stored, 16)
            sp.wait_ge(stored, 16 * PAIRS)

        @block.gpsimd
        def _(pool):
            nc.gpsimd.memset(head_mask[:, :], 1.0).then_inc(mask_zeroed, 1)
            nc.gpsimd.memset(identity[:, :, :], 0.0).then_inc(mask_zeroed, 1)
            pool.wait_ge(mask_zeroed, 2)
            blocks = head_mask[:, :].rearrange("p (h d) -> p h d", d=D)
            nc.gpsimd.affine_select(out=blocks, in_=blocks, compare_op=ALU.is_ge, fill=0.0, base=0,
                                    pattern=[[-D, HEADS], [0, D]], channel_multiplier=1).then_inc(mask_zeroed, 1)
            pool.wait_ge(mask_zeroed, 3)
            nc.gpsimd.affine_select(out=blocks, in_=blocks, compare_op=ALU.is_ge, fill=0.0, base=D - 1,
                                    pattern=[[D, HEADS], [0, D]], channel_multiplier=-1).then_inc(consts_ready, 1)
            nc.gpsimd.affine_select(out=identity[:, :, :], in_=identity[:, :, :], compare_op=ALU.not_equal,
                                    fill=1.0, base=0, pattern=[[0, 2], [-1, C]],
                                    channel_multiplier=1).then_inc(consts_ready, 1)

            def split_lo(p):
                pool.wait_ge(x_hi_ready, p + 1)
                nc.gpsimd.tensor_tensor(x_lo[:, p, :], x_sb[:, p, :], x_hi[:, p, :].bitcast(F32),
                                        ALU.subtract).then_inc(x_lo_ready, 1)

            def normalise(p):
                pool.wait_ge(inv_ready, p + 1)
                inv = k_inv[:, p, :].rearrange("n (g o) -> n g o", o=1).to_broadcast([128, 2 * CH * HEADS, D])
                heads = probs[:, p].rearrange("n g (h d) -> n (g h) d", d=D)
                nc.gpsimd.tensor_tensor(heads, heads, inv, ALU.mult).then_inc(probs_ready, 1)

            run_slots((normalise, 1), (split_lo, -1))

        @block.scalar
        def _(act):
            def split_hi(p):
                for i, (lo, hi) in enumerate(PIECES):
                    if p == lo:
                        act.wait_ge(x_landed[i], 16)
                nc.scalar.activation(x_hi[:, p, :], x_sb[:, p, :], ACT.Copy).then_inc(x_hi_ready, 1)

            def exponentials(p):
                act.wait_ge(shift_ready, p + 1)
                nc.scalar.activation(probs[:, p], probs[:, p], ACT.Exp).then_inc(exp_ready, 1)

            def copy_values(p):
                nc.scalar.activation(v_sb[:, p], kv_ps[:, p % 2, :, C:2 * C], ACT.Copy).then_inc(v_ready, 1)

            def copy_u(p):
                act.wait_ge(u_ready, p + 1)
                nc.scalar.activation(u_sb[:, p, :], u_ps[:, 0:2 * C], ACT.Copy).then_inc(u_copied, 1)

            def split_a_hi(p):
                act.wait_ge(a_ready, p + 1)
                nc.scalar.activation(a_hi[:, p, :], a_ps[:, 0:2 * C], ACT.Copy).then_inc(a_hi_ready, 1)

            def copy_y(p):
                act.wait_ge(y_ready, p + 1)
                nc.scalar.activation(y_sb[:, p, :], y_ps[:, :], ACT.Copy).then_inc(y_copied, 1)

            run_slots((exponentials, 1), (copy_y, 4), (copy_values, 1), (copy_u, 2), (split_hi, -1), (split_a_hi, 2))
            act.wait_ge(final_step, 2)
            nc.scalar.activation(std[:, :], var_eps[:, :], ACT.Sqrt).then_inc(std_ready, 1)
            act.wait_ge(affine_ready, 1)
            for p in LAST_OF_SCALAR:
                seg = y_sb[:, p, :]
                nc.scalar.activation(seg, seg, ACT.Identity, bias=shift[:, 0:1],
                                     scale=scale[:, 0:1]).then_inc(out_by_scalar, 1)

        @block.vector
        def _(dve):
            dve.wait_ge(w_landed, 16)
            nc.vector.tensor_copy(wkv_hi[:, :], wkv).then_inc(w_hi_ready, 1)
            dve.wait_ge(w_hi_ready, 1)
            nc.vector.tensor_tensor(wkv_lo[:, :], wkv, wkv_hi[:, :].bitcast(F32), ALU.subtract).then_inc(w_lo_ready, 1)

            def shift_keys(p):
                keys = kv_ps[:, p % 2, :, 0:C].rearrange("n g (h d) -> n g h d", d=D)
                dve.wait_ge(kv_ready, p + 1)
                nc.vector.tensor_reduce(k_max[:, p, :], keys, AX.X, ALU.max).then_inc(max_ready, 1)
                dve.wait_ge(max_ready, p + 1)
                largest = k_max[:, p, :].rearrange("n (g h o) -> n g h o", g=2 * CH, o=1)
                nc.vector.tensor_tensor(probs[:, p].rearrange("n g (h d) -> n g h d", d=D), keys,
                                        largest.to_broadcast([128, 2 * CH, HEADS, D]),
                                        ALU.subtract).then_inc(shift_ready, 1)

            def sum_heads(p):
                dve.wait_ge(exp_ready, p + 1)
                nc.vector.tensor_reduce(k_sum[:, p, :], probs[:, p].rearrange("n g (h d) -> n (g h) d", d=D),
                                        AX.X, ALU.add).then_inc(sum_ready, 1)
                dve.wait_ge(sum_ready, p + 1)
                nc.vector.reciprocal(k_inv[:, p, :], k_sum[:, p, :]).then_inc(inv_ready, 1)

            def mask_context(p):
                dve.wait_ge(ct_ready, p + 1)
                if p == 0:
                    dve.wait_ge(consts_ready, 2)
                nc.vector.tensor_tensor(ct_sb[:, p], ct_ps[:, 0:2 * C].rearrange("e (b d) -> e b d", b=2),
                                        head_mask[:, :].rearrange("e (o d) -> e o d", o=1).to_broadcast([C, 2, C]),
                                        ALU.mult).then_inc(ct_masked, 1)

            def split_a_lo(p):
                dve.wait_ge(a_hi_ready, p + 1)
                nc.vector.tensor_tensor(a_lo[:, p, :], a_ps[:, 0:2 * C], a_hi[:, p, :].bitcast(F32),
                                        ALU.subtract).then_inc(a_lo_ready, 1)

            def count_y(p):
                dve.wait_ge(y_copied, p + 1)
                nc.vector.bn_stats(stats[:, p * 6:(p + 1) * 6], y_sb[:, p, :]).then_inc(y_counted, 1)

            run_slots((sum_heads, 1), (mask_context, 2), (count_y, 4), (shift_keys, 0), (split_a_lo, 2))
            dve.wait_ge(y_counted, PAIRS)
            nc.vector.bn_aggr(mean_var[:, :], stats[:, :]).then_inc(final_step, 1)
            dve.wait_ge(final_step, 1)
            nc.vector.tensor_scalar(var_eps[:, :], mean_var[:, 1:2], EPS, None, ALU.add).then_inc(final_step, 1)
            dve.wait_ge(std_ready, 1)
            nc.vector.reciprocal(rstd[:, :], std[:, :]).then_inc(final_step, 1)
            dve.wait_ge(final_step, 3)
            dve.wait_ge(affine_landed, 16)
            nc.vector.tensor_tensor(scale[:, :], rstd[:, :], gamma_beta[:, 0:1], ALU.mult).then_inc(final_step, 1)
            dve.wait_ge(final_step, 4)
            nc.vector.tensor_tensor(mean_scale[:, :], mean_var[:, 0:1], scale[:, :], ALU.mult).then_inc(final_step, 1)
            dve.wait_ge(final_step, 5)
            nc.vector.tensor_tensor(shift[:, :], gamma_beta[:, 1:2], mean_scale[:, :],
                                    ALU.subtract).then_inc(affine_ready, 1)
            dve.wait_ge(affine_ready, 1)
            dve.wait_ge(y_copied, PAIRS)
            for p in LAST_OF_VECTOR:
                seg = y_sb[:, p, :]
                nc.vector.tensor_scalar(seg, seg, scale[:, 0:1], shift[:, 0:1], ALU.mult,
                                        ALU.add).then_inc(out_by_vector, 1)

        @block.tensor
        def _(pe):
            def project(p, image):
                if image == 0:
                    pe.wait_ge(x_hi_ready, p + 1)
                    if p >= 2:
                        pe.wait_ge(v_ready, p - 1)
                    if p == 0:
                        pe.wait_ge(w_lo_ready, 1)
                    pe.wait_ge(x_lo_ready, p + 1)
                for g in range(CH * image, CH * image + CH):
                    px = slice(g * 128, (g + 1) * 128)
                    kv = kv_ps[:, p % 2, g, :]
                    nc.tensor.matmul(kv, x_hi[:, p, px], wkv_hi[:, :], start=True, stop=False)
                    nc.tensor.matmul(kv, x_hi[:, p, px], wkv_lo[:, :], start=False, stop=False)
                    last = nc.tensor.matmul(kv, x_lo[:, p, px], wkv_hi[:, :], start=False, stop=True)
                if image == 1:
                    last.then_inc(kv_ready, 1)

            def context(p):
                pe.wait_ge(probs_ready, p + 1)
                pe.wait_ge(v_ready, p + 1)
                if p >= 1:
                    pe.wait_ge(ct_masked, p)
                for image in range(2):
                    for g in range(CH):
                        last = nc.tensor.matmul(ct_ps[:, image * C:(image + 1) * C], v_sb[:, p, image * CH + g, :],
                                                probs[:, p, image * CH + g, :], start=(g == 0), stop=(g == CH - 1))
                last.then_inc(ct_ready, 1)

            def times_wo(p):
                pe.wait_ge(ct_masked, p + 1)
                if p >= 1:
                    pe.wait_ge(u_copied, p)
                for image in range(2):
                    last = nc.tensor.matmul(u_ps[:, image * C:(image + 1) * C], ct_sb[:, p, image, :], woT,
                                            start=True, stop=True)
                last.then_inc(u_ready, 1)

            def times_wq(p):
                if p >= 1:
                    pe.wait_ge(a_lo_ready, p)
                if p == 0:
                    pe.wait_ge(consts_ready, 2)
                nc.tensor.matmul(a_ps[:, 0:2 * C], identity[:, 0, :], identity[:, :, :].rearrange("c b o -> c (b o)"),
                                 start=True, stop=False)
                pe.wait_ge(u_copied, p + 1)
                nc.tensor.matmul(a_ps[:, 0:2 * C], wq, u_sb[:, p, :], start=False, stop=True).then_inc(a_ready, 1)

            def apply(p):
                pe.wait_ge(a_hi_ready, p + 1)
                if p >= 1:
                    pe.wait_ge(y_copied, p)
                pe.wait_ge(a_lo_ready, p + 1)
                for image in range(2):
                    y = y_ps[:, image * N:(image + 1) * N]
                    cols, px = slice(image * C, (image + 1) * C), slice(image * N, (image + 1) * N)
                    nc.tensor.matmul(y, a_hi[:, p, cols], x_hi[:, p, px], start=True, stop=False)
                    nc.tensor.matmul(y, a_hi[:, p, cols], x_lo[:, p, px], start=False, stop=False)
                    last = nc.tensor.matmul(y, a_lo[:, p, cols], x_hi[:, p, px], start=False, stop=True)
                last.then_inc(y_ready, 1)

            run_slots((context, 2), (lambda p: project(p, 0), 0), (times_wo, 2), (lambda p: project(p, 1), 0),
                      (times_wq, 2), (apply, 3))


def kernel(x, L0_conv_Wq, L0_conv_Wk, L0_conv_Wv, L0_conv_Wo, L0_conv_gamma, L0_conv_beta):
    import numpy as np
    import concourse.bacc as bacc
    from concourse.bass_utils import run_bass_kernel_spmd

    x = np.asarray(x)
    shape = x.shape
    arrays = {
        "x_dram": np.ascontiguousarray(x).reshape(B, C, N),
        "w_dram": np.concatenate([np.asarray(L0_conv_Wk).T, np.asarray(L0_conv_Wv).T,
                                  np.asarray(L0_conv_Wq), np.asarray(L0_conv_Wo).T], axis=1),
        "affine_dram": np.stack([np.asarray(L0_conv_gamma), np.asarray(L0_conv_beta)], axis=1),
    }
    nc = bacc.Bacc("TRN2", target_bir_lowering=False, num_devices=1)
    args = [nc.dram_tensor(n, a.shape, mybir.dt.from_np(a.dtype), kind="ExternalInput").ap()
            for n, a in arrays.items()]
    args.append(nc.dram_tensor("out_dram", (B, C, N), F32, kind="ExternalOutput").ap())
    attention_batchnorm(nc, *args)
    result = run_bass_kernel_spmd(nc, [arrays], core_ids=[0])
    return result.results[0]["out_dram"].reshape(shape)
```

```python
from contextlib import ExitStack

import concourse.bass as bass
from concourse import mybir

ALU = mybir.AluOpType
ACT = mybir.ActivationFunctionType
AX = mybir.AxisListType
F32 = mybir.dt.float32
F32R = mybir.dt.float32r
BF16 = mybir.dt.bfloat16

B = 16
C = 128
N = 256
HEADS = 8
D = C // HEADS
CH = N // 128
PAIRS = B // 2
PN = 2 * N
EPS = 1e-5


def attention_batchnorm(nc: bass.Bass, x, w, affine, out):
    with ExitStack() as ctx:
        def sb(name, shape, dt=F32):
            return ctx.enter_context(nc.sbuf_tensor(name, shape, dt))

        def ps(name, shape, dt=F32):
            return ctx.enter_context(nc.psum_tensor(name, shape, dt))

        def sem(name):
            return ctx.enter_context(nc.semaphore(name))

        w_sb = sb("w_sb", [C, 4 * C])
        wkv = w_sb[:, 0:2 * C]
        wq = w_sb[:, 2 * C:3 * C]
        woT = w_sb[:, 3 * C:4 * C]
        wkv_hi = sb("wkv_hi", [C, 2 * C], F32R)
        wkv_lo = sb("wkv_lo", [C, 2 * C], F32R)
        head_mask = sb("head_mask", [C, C])
        identity = sb("identity", [C, 2, C], BF16)
        gamma_beta = sb("gamma_beta", [C, 2])
        x_sb = sb("x_sb", [C, PAIRS, PN])
        y_sb = sb("y_sb", [C, PAIRS, PN])
        x_hi = sb("x_hi", [C, PAIRS, PN], F32R)
        x_lo = sb("x_lo", [C, PAIRS, PN], F32R)
        k_max = sb("k_max", [128, PAIRS, 2, CH * HEADS])
        probs = sb("probs", [128, PAIRS, 2 * CH, C])
        k_sum = sb("k_sum", [128, PAIRS, 2, CH * HEADS])
        k_inv = sb("k_inv", [128, PAIRS, 2, CH * HEADS])
        v_sb = sb("v_sb", [128, PAIRS, 2 * CH, C])
        ct_sb = sb("ct_sb", [C, PAIRS, 2, C])
        u_sb = sb("u_sb", [C, PAIRS, 2 * C])
        a_hi = sb("a_hi", [C, PAIRS, 2 * C], F32R)
        a_lo = sb("a_lo", [C, PAIRS, 2 * C], F32R)
        stats = sb("stats", [C, PAIRS * 6])
        mean_var = sb("mean_var", [C, 2])
        eps = sb("eps", [C, 1])
        std = sb("std", [C, 1])
        rstd = sb("rstd", [C, 1])
        scale = sb("scale", [C, 1])
        shift = sb("shift", [C, 1])

        kv_ps = ps("kv_ps", [128, 2, 2 * CH, 2 * C])
        ct_ps = ps("ct_ps", [C, 512])
        u_ps = ps("u_ps", [C, 512])
        a_ps = ps("a_ps", [C, 512])
        y_ps = ps("y_ps", [C, PN])

        wkv_landed = sem("wkv_landed")
        wqo_landed = sem("wqo_landed")
        eps_set = sem("eps_set")
        affine_landed = sem("affine_landed")
        x_landed = [sem(f"x_landed{i}") for i in range(6)]
        mask_zeroed = sem("mask_zeroed")
        consts_ready = sem("consts_ready")
        w_hi_ready = sem("w_hi_ready")
        w_lo_ready = sem("w_lo_ready")
        x_hi_ready = sem("x_hi_ready")
        x_lo_ready = sem("x_lo_ready")
        first_lo_ready = sem("first_lo_ready")
        kv_ready = sem("kv_ready")
        max_ready = sem("max_ready")
        shift_ready = sem("shift_ready")
        exp_ready = sem("exp_ready")
        sum_ready = sem("sum_ready")
        inv_ready = sem("inv_ready")
        probs_ready = sem("probs_ready")
        v_ready = sem("v_ready")
        ct_ready = sem("ct_ready")
        ct_masked = sem("ct_masked")
        u_ready = sem("u_ready")
        u_copied = sem("u_copied")
        a_ready = sem("a_ready")
        a_hi_ready = sem("a_hi_ready")
        a_lo_ready = sem("a_lo_ready")
        y_ready = sem("y_ready")
        y_copied = sem("y_copied")
        y_counted = sem("y_counted")
        aggregated = sem("aggregated")
        rstd_ready = sem("rstd_ready")
        scale_ready = sem("scale_ready")
        shift_final = sem("shift_final")
        std_ready = sem("std_ready")
        out_by_vector = sem("out_by_vector")
        out_by_scalar = sem("out_by_scalar")
        stored = sem("stored")

        PIECES = [(0, 1), (1, 2), (2, 4), (4, 6), (6, 8), (8, 16)]
        x_view = x_sb[:, :, :].rearrange("c p (b n) -> c (p b) n", n=N)
        y_view = y_sb[:, :, :].rearrange("c p (b n) -> c (p b) n", n=N)
        y_all = y_sb[:, :, :].rearrange("c p n -> c (p n)")
        BY_VECTOR = [(0, N), (N, PN), (PN, 2 * PN), (3 * PN, 4 * PN), (4 * PN, 5 * PN), (5 * PN, 6 * PN)]
        BY_SCALAR = [2, 7, 6]
        STORES = [(0, 1, 1, 0), (1, 4, 3, 0), (4, 6, 0, 1), (6, 8, 4, 0), (8, 12, 6, 0), (12, 16, 0, 3)]
        LAG_C, LAG_A, LAG_Y = 2, 3, 4
        WARM_UP = 8
        AHEAD = 3
        BY_POOL = 2

        def parts(p):
            return [(0, 1), (1, 2)] if p == 0 else [(0, 2)]

        def run_slots(*stages):
            for t in range(-2, PAIRS + 6):
                for stage, lag in stages:
                    if 0 <= t - lag < PAIRS:
                        stage(t - lag)

        def y_bank(p):
            if p < PAIRS - 2:
                return y_ps[:, :]
            return kv_ps[:, p % 2, 0:CH, :].rearrange("c g n -> c (g n)")

        block = ctx.enter_context(nc.Block())

        @block.sync
        def _(sp):
            sp.dma_start(w_sb[:, 0:2 * C], w[:, 0:2 * C]).then_inc(wkv_landed, 16)
            for i, (lo, hi) in enumerate(PIECES):
                sp.dma_start(x_view[:, lo:hi, :], x[lo:hi].rearrange("b c n -> c b n")).then_inc(x_landed[i], 16)
                if i == 3:
                    sp.dma_start(w_sb[:, 2 * C:4 * C], w[:, 2 * C:4 * C]).then_inc(wqo_landed, 16)
            sp.dma_start(gamma_beta[:, :], affine).then_inc(affine_landed, 16)
            for lo, hi, vector_steps, scalar_steps in STORES:
                if vector_steps:
                    sp.wait_ge(out_by_vector, vector_steps)
                if scalar_steps:
                    sp.wait_ge(out_by_scalar, scalar_steps)
                sp.dma_start(out[lo:hi].rearrange("b c n -> c b n"), y_view[:, lo:hi, :]).then_inc(stored, 16)
            sp.wait_ge(stored, 16 * len(STORES))

        @block.gpsimd
        def _(pool):
            nc.gpsimd.memset(head_mask[:, :], 1.0).then_inc(mask_zeroed, 1)
            nc.gpsimd.memset(identity[:, :, :], 0.0).then_inc(mask_zeroed, 1)
            pool.wait_ge(mask_zeroed, 2)
            blocks = head_mask[:, :].rearrange("p (h d) -> p h d", d=D)
            nc.gpsimd.affine_select(out=blocks, in_=blocks, compare_op=ALU.is_ge, fill=0.0, base=0,
                                    pattern=[[-D, HEADS], [0, D]], channel_multiplier=1).then_inc(mask_zeroed, 1)
            pool.wait_ge(mask_zeroed, 3)
            nc.gpsimd.affine_select(out=blocks, in_=blocks, compare_op=ALU.is_ge, fill=0.0, base=D - 1,
                                    pattern=[[D, HEADS], [0, D]], channel_multiplier=-1).then_inc(consts_ready, 1)
            nc.gpsimd.affine_select(out=identity[:, :, :], in_=identity[:, :, :], compare_op=ALU.not_equal,
                                    fill=1.0, base=0, pattern=[[0, 2], [-1, C]],
                                    channel_multiplier=1).then_inc(consts_ready, 1)

            def split_lo(p):
                pool.wait_ge(x_hi_ready, 2 * (p + 1))
                nc.gpsimd.tensor_tensor(x_lo[:, p, :], x_sb[:, p, :], x_hi[:, p, :].bitcast(F32),
                                        ALU.subtract).then_inc(x_lo_ready, 1)

            def normalise(p):
                for lo, hi in parts(p):
                    pool.wait_ge(inv_ready, 2 * p + hi)
                    inv = k_inv[:, p, lo:hi, :].rearrange("n i (g o) -> n (i g) o", o=1)
                    heads = probs[:, p, CH * lo:CH * hi].rearrange("n g (h d) -> n (g h) d", d=D)
                    nc.gpsimd.tensor_tensor(heads, heads, inv.to_broadcast([128, (hi - lo) * CH * HEADS, D]),
                                            ALU.mult).then_inc(probs_ready, hi - lo)

            for p in range(BY_POOL, AHEAD):
                split_lo(p)
            run_slots((normalise, 0), (lambda p: split_lo(p) if p >= AHEAD else None, -AHEAD))

        @block.scalar
        def _(act):
            def split_hi(p):
                for i, (lo, hi) in enumerate(PIECES):
                    if lo == 2 * p:
                        act.wait_ge(x_landed[i], 16)
                nc.scalar.activation(x_hi[:, p, :], x_sb[:, p, :], ACT.Copy).then_inc(x_hi_ready, 2)

            for image in range(2):
                act.wait_ge(x_landed[image], 16)
                px = slice(image * N, (image + 1) * N)
                nc.scalar.activation(x_hi[:, 0, px], x_sb[:, 0, px], ACT.Copy).then_inc(x_hi_ready, 1)
            for p in range(1, AHEAD):
                split_hi(p)

            def exponentials(p):
                for lo, hi in parts(p):
                    act.wait_ge(shift_ready, 2 * p + hi)
                    chunks = probs[:, p, CH * lo:CH * hi]
                    nc.scalar.activation(chunks, chunks, ACT.Exp).then_inc(exp_ready, hi - lo)

            def copy_values(p):
                for lo, hi in parts(p):
                    chunks = slice(CH * lo, CH * hi)
                    nc.scalar.activation(v_sb[:, p, chunks], kv_ps[:, p % 2, chunks, C:2 * C],
                                         ACT.Copy).then_inc(v_ready, hi - lo)

            def copy_u(p):
                act.wait_ge(u_ready, p + 1)
                nc.scalar.activation(u_sb[:, p, :], u_ps[:, 0:2 * C], ACT.Copy).then_inc(u_copied, 1)

            def split_a_hi(p):
                act.wait_ge(a_ready, p + 1)
                nc.scalar.activation(a_hi[:, p, :], a_ps[:, 0:2 * C], ACT.Copy).then_inc(a_hi_ready, 1)

            def copy_y(p):
                act.wait_ge(y_ready, p + 1)
                nc.scalar.activation(y_sb[:, p, :], y_bank(p), ACT.Copy).then_inc(y_copied, 1)

            def copy_y_but_last(p):
                if p < PAIRS - 1:
                    copy_y(p)

            run_slots((split_a_hi, LAG_A), (exponentials, 0), (copy_u, LAG_C), (copy_y_but_last, LAG_Y), (copy_values, 0),
                      (lambda p: split_hi(p) if p >= AHEAD else None, -AHEAD))
            act.wait_ge(aggregated, 1)
            nc.scalar.activation(std[:, :], mean_var[:, 1:2], ACT.Sqrt, bias=eps[:, 0:1]).then_inc(std_ready, 1)
            act.wait_ge(shift_final, 1)
            for p in BY_SCALAR:
                nc.scalar.activation(y_sb[:, p, :], y_sb[:, p, :] if p < PAIRS - 1 else y_bank(p), ACT.Identity,
                                     bias=shift[:, 0:1], scale=scale[:, 0:1]).then_inc(out_by_scalar, 1)

        @block.vector
        def _(dve):
            nc.vector.memset(eps[:, :], EPS).then_inc(eps_set, 1)
            dve.wait_ge(wkv_landed, 16)
            nc.vector.tensor_copy(wkv_hi[:, :], wkv).then_inc(w_hi_ready, 1)
            dve.wait_ge(w_hi_ready, 1)
            nc.vector.tensor_tensor(wkv_lo[:, :], wkv, wkv_hi[:, :].bitcast(F32), ALU.subtract).then_inc(w_lo_ready, 1)

            for p in range(BY_POOL):
                for lo, hi in parts(p):
                    dve.wait_ge(x_hi_ready, 2 * p + hi)
                    px = slice(lo * N, hi * N)
                    nc.vector.tensor_tensor(x_lo[:, p, px], x_sb[:, p, px], x_hi[:, p, px].bitcast(F32),
                                            ALU.subtract).then_inc(first_lo_ready, hi - lo)

            def keys(p, lo, hi):
                return kv_ps[:, p % 2, CH * lo:CH * hi, 0:C].rearrange("n g (h d) -> n g h d", d=D)

            def largest_keys(p):
                for lo, hi in parts(p):
                    dve.wait_ge(kv_ready, 2 * p + hi)
                    nc.vector.tensor_reduce(k_max[:, p, lo:hi, :], keys(p, lo, hi), AX.X, ALU.max
                                            ).then_inc(max_ready, hi - lo)

            def shift_keys(p):
                for lo, hi in parts(p):
                    dve.wait_ge(max_ready, 2 * p + hi)
                    largest = k_max[:, p, lo:hi, :].rearrange("n i (g h o) -> n (i g) h o", g=CH, o=1)
                    nc.vector.tensor_tensor(probs[:, p, CH * lo:CH * hi].rearrange("n g (h d) -> n g h d", d=D),
                                            keys(p, lo, hi), largest.to_broadcast([128, (hi - lo) * CH, HEADS, D]),
                                            ALU.subtract).then_inc(shift_ready, hi - lo)

            def sum_heads(p):
                for lo, hi in parts(p):
                    dve.wait_ge(exp_ready, 2 * p + hi)
                    nc.vector.tensor_reduce(k_sum[:, p, lo:hi, :],
                                            probs[:, p, CH * lo:CH * hi].rearrange("n g (h d) -> n (g h) d", d=D),
                                            AX.X, ALU.add).then_inc(sum_ready, hi - lo)

            def invert_sums(p):
                for lo, hi in parts(p):
                    dve.wait_ge(sum_ready, 2 * p + hi)
                    nc.vector.reciprocal(k_inv[:, p, lo:hi, :], k_sum[:, p, lo:hi, :]).then_inc(inv_ready, hi - lo)

            def mask_context(p):
                dve.wait_ge(ct_ready, p + 1)
                if p == 0:
                    dve.wait_ge(consts_ready, 2)
                nc.vector.tensor_tensor(ct_sb[:, p], ct_ps[:, 0:2 * C].rearrange("e (b d) -> e b d", b=2),
                                        head_mask[:, :].rearrange("e (o d) -> e o d", o=1).to_broadcast([C, 2, C]),
                                        ALU.mult).then_inc(ct_masked, 1)

            def split_a_lo(p):
                dve.wait_ge(a_hi_ready, p + 1)
                nc.vector.tensor_tensor(a_lo[:, p, :], a_ps[:, 0:2 * C], a_hi[:, p, :].bitcast(F32),
                                        ALU.subtract).then_inc(a_lo_ready, 1)

            def count_y(p):
                if p < PAIRS - 1:
                    dve.wait_ge(y_copied, p + 1)
                else:
                    dve.wait_ge(y_ready, p + 1)
                nc.vector.bn_stats(stats[:, p * 6:(p + 1) * 6], y_sb[:, p, :] if p < PAIRS - 1 else y_bank(p)
                                   ).then_inc(y_counted, 1)

            run_slots((largest_keys, 0), (sum_heads, 1), (mask_context, LAG_C), (invert_sums, 1), (shift_keys, 0),
                      (split_a_lo, LAG_A), (count_y, LAG_Y + 1))
            dve.wait_ge(y_counted, PAIRS)
            nc.vector.bn_aggr(mean_var[:, :], stats[:, :]).then_inc(aggregated, 1)
            dve.wait_ge(std_ready, 1)
            nc.vector.reciprocal(rstd[:, :], std[:, :]).then_inc(rstd_ready, 1)
            dve.wait_ge(rstd_ready, 1)
            dve.wait_ge(affine_landed, 16)
            nc.vector.tensor_tensor(scale[:, :], rstd[:, :], gamma_beta[:, 0:1], ALU.mult).then_inc(scale_ready, 1)
            dve.wait_ge(scale_ready, 1)
            nc.vector.scalar_tensor_tensor(out=shift[:, :], in0=mean_var[:, 0:1], scalar=scale[:, 0:1],
                                           in1=gamma_beta[:, 1:2], op0=ALU.mult, op1=ALU.subtract,
                                           reverse1=True).then_inc(shift_final, 1)
            dve.wait_ge(shift_final, 1)
            dve.wait_ge(y_copied, PAIRS - 1)
            for lo, hi in BY_VECTOR:
                seg = y_all[:, lo:hi]
                nc.vector.tensor_scalar(seg, seg, scale[:, 0:1], shift[:, 0:1], ALU.mult,
                                        ALU.add).then_inc(out_by_vector, 1)

        @block.tensor
        def _(pe):
            def project(p):
                if p == 0:
                    pe.wait_ge(w_hi_ready, 1)
                for image in range(2):
                    in_halves = 2 * p + (image + 1 if p == 0 else 2)
                    pe.wait_ge(x_hi_ready, in_halves)
                    if p >= 2:
                        pe.wait_ge(v_ready, 2 * (p - 2) + (image + 1 if p == 2 else 2))

                    def pass_over(xs, ws, start, stop):
                        for g in range(CH * image, CH * image + CH):
                            last = nc.tensor.matmul(kv_ps[:, p % 2, g, :], xs[:, p, g * 128:(g + 1) * 128], ws[:, :],
                                                    start=start and g == CH * image, stop=stop, skip_group_check=True)
                        return last

                    pass_over(x_hi, wkv_hi, True, False)
                    if p == 0:
                        pe.wait_ge(w_lo_ready, 1)
                    pass_over(x_hi, wkv_lo, False, False)
                    if p < BY_POOL:
                        pe.wait_ge(first_lo_ready, in_halves)
                    else:
                        pe.wait_ge(x_lo_ready, p - BY_POOL + 1)
                    pass_over(x_lo, wkv_hi, False, True).then_inc(kv_ready, 1)

            def context(p):
                pe.wait_ge(probs_ready, 2 * (p + 1))
                pe.wait_ge(v_ready, 2 * (p + 1))
                if p >= 1:
                    pe.wait_ge(ct_masked, p)
                for image in range(2):
                    for g in range(CH):
                        last = nc.tensor.matmul(ct_ps[:, image * C:(image + 1) * C], v_sb[:, p, image * CH + g, :],
                                                probs[:, p, image * CH + g, :], start=(g == 0), stop=(g == CH - 1))
                last.then_inc(ct_ready, 1)

            def times_wo(p):
                if p == 0:
                    pe.wait_ge(wqo_landed, 16)
                pe.wait_ge(ct_masked, p + 1)
                if p >= 1:
                    pe.wait_ge(u_copied, p)
                for image in range(2):
                    last = nc.tensor.matmul(u_ps[:, image * C:(image + 1) * C], ct_sb[:, p, image, :], woT,
                                            start=True, stop=True)
                last.then_inc(u_ready, 1)

            def times_wq(p):
                if p >= 1:
                    pe.wait_ge(a_lo_ready, p)
                if p == 0:
                    pe.wait_ge(consts_ready, 2)
                nc.tensor.matmul(a_ps[:, 0:2 * C], identity[:, 0, :], identity[:, :, :].rearrange("c b o -> c (b o)"),
                                 start=True, stop=False)
                pe.wait_ge(u_copied, p + 1)
                nc.tensor.matmul(a_ps[:, 0:2 * C], wq, u_sb[:, p, :], start=False, stop=True).then_inc(a_ready, 1)

            def apply(p):
                pe.wait_ge(a_hi_ready, p + 1)
                if 1 <= p < PAIRS - 2:
                    pe.wait_ge(y_copied, p)
                def pass_over(a, xs, start, stop):
                    for image in range(2):
                        last = nc.tensor.matmul(y_bank(p)[:, image * N:(image + 1) * N],
                                                a[:, p, image * C:(image + 1) * C], xs[:, p, image * N:(image + 1) * N],
                                                start=start and image == 0, stop=stop, skip_group_check=True)
                    return last

                pass_over(a_hi, x_hi, True, False)
                pass_over(a_hi, x_lo, False, False)
                pe.wait_ge(a_lo_ready, p + 1)
                last = pass_over(a_lo, x_hi, False, True)
                last.then_inc(y_ready, 1)

            zeros = nc.const_aps.tensor(0.0, [128, 128], F32)
            for _ in range(WARM_UP):
                nc.tensor.matmul(y_ps[:, 0:128], zeros, zeros, start=True, stop=True)

            run_slots((project, 0), (context, LAG_C), (lambda p: times_wq(p) if p < PAIRS - 1 else None, LAG_A),
                      (lambda p: apply(p) if p < PAIRS - 1 else None, LAG_Y), (times_wo, LAG_C))
            times_wq(PAIRS - 1)
            apply(PAIRS - 1)


def kernel(x, L0_conv_Wq, L0_conv_Wk, L0_conv_Wv, L0_conv_Wo, L0_conv_gamma, L0_conv_beta):
    import numpy as np
    import concourse.bacc as bacc
    from concourse.bass_utils import run_bass_kernel_spmd

    x = np.asarray(x)
    shape = x.shape
    arrays = {
        "x_dram": np.ascontiguousarray(x).reshape(B, C, N),
        "w_dram": np.concatenate([np.asarray(L0_conv_Wk).T, np.asarray(L0_conv_Wv).T,
                                  np.asarray(L0_conv_Wq), np.asarray(L0_conv_Wo).T], axis=1),
        "affine_dram": np.stack([np.asarray(L0_conv_gamma), np.asarray(L0_conv_beta)], axis=1),
    }
    nc = bacc.Bacc("TRN2", target_bir_lowering=False, num_devices=1)
    args = [nc.dram_tensor(n, a.shape, mybir.dt.from_np(a.dtype), kind="ExternalInput").ap()
            for n, a in arrays.items()]
    args.append(nc.dram_tensor("out_dram", (B, C, N), F32, kind="ExternalOutput").ap())
    attention_batchnorm(nc, *args)
    result = run_bass_kernel_spmd(nc, [arrays], core_ids=[0])
    return result.results[0]["out_dram"].reshape(shape)
```

```python
from contextlib import ExitStack

import concourse.bass as bass
from concourse import mybir

ALU = mybir.AluOpType
ACT = mybir.ActivationFunctionType
AX = mybir.AxisListType
F32 = mybir.dt.float32
F32R = mybir.dt.float32r
BF16 = mybir.dt.bfloat16

B = 16
C = 128
N = 256
HEADS = 8
D = C // HEADS
CH = N // 128
T = 64
PAIRS = B // 2
PN = 2 * N
EPS = 1e-5

EXTRA = 2
LAST = PAIRS - 1
IN_PSUM = PAIRS - 3
LO_BY_VECTOR = 2
WARM_UP = 7
STORES = [
    (0, 1, [("vector", 0, 1)]),
    (4, 6, [("vector", 4, 6)]),
    (1, 2, [("vector", 1, 2)]),
    (8, 12, [("vector", 8, 10), ("scalar", 10, 12)]),
    (2, 4, [("vector", 2, 4)]),
    (12, 16, [("vector", 12, 14), ("vector", 14, 16)]),
    (6, 8, [("scalar", 6, 8)]),
]


def attention_batchnorm(nc: bass.Bass, x, w, affine, out):
    with ExitStack() as ctx:
        def sb(name, shape, dt=F32):
            return ctx.enter_context(nc.sbuf_tensor(name, shape, dt))

        def ps(name, shape, dt=F32):
            return ctx.enter_context(nc.psum_tensor(name, shape, dt))

        def sem(name):
            return ctx.enter_context(nc.semaphore(name))

        w_sb = sb("w_sb", [C, 4 * C])
        wkv = w_sb[:, 0:2 * C]
        wq = w_sb[:, 2 * C:3 * C]
        woT = w_sb[:, 3 * C:4 * C]
        wkv_hi = sb("wkv_hi", [C, 2 * C], F32R)
        wkv_lo = sb("wkv_lo", [C, 2 * C], F32R)
        same_head = sb("same_head", [C, C])
        head_mask = sb("head_mask", [C, T])
        identity = sb("identity", [C, 2, C], BF16)
        gamma_beta = sb("gamma_beta", [C, 2])
        x_sb = sb("x_sb", [C, PAIRS, PN])
        y_sb = sb("y_sb", [C, PAIRS, PN])
        x_hi = sb("x_hi", [C, PAIRS, PN], F32R)
        x_lo = sb("x_lo", [C, PAIRS, PN], F32R)
        k_max = sb("k_max", [128, PAIRS, 2, CH * HEADS])
        probs = sb("probs", [128, PAIRS, 2 * CH, C])
        k_sum = sb("k_sum", [128, PAIRS, 2, CH * HEADS])
        k_inv = sb("k_inv", [128, PAIRS, 2, CH * HEADS])
        v_sb = sb("v_sb", [128, PAIRS, 2 * CH, C])
        ct_sb = sb("ct_sb", [C, PAIRS, 2, T])
        u_sb = sb("u_sb", [C, PAIRS, 2 * C])
        a_hi = sb("a_hi", [C, PAIRS, 2 * C], F32R)
        a_lo = sb("a_lo", [C, PAIRS, 2 * C], F32R)
        stats = sb("stats", [C, (PAIRS + 1) * 6])
        mean_var = sb("mean_var", [C, 2])
        eps = sb("eps", [C, 1])
        std = sb("std", [C, 1])
        rstd = sb("rstd", [C, 1])
        mean_gamma = sb("mean_gamma", [C, 1])
        scale = sb("scale", [C, 1])
        shift = sb("shift", [C, 1])

        banks = ps("banks", [128, 8, 512])

        def kv_bank(p):
            return 6 if p == EXTRA else 2 * ((p - (p > EXTRA)) % 2)

        def kv_before(p):
            return max((q for q in range(p) if kv_bank(q) == kv_bank(p)), default=None)

        def kv_ps(p):
            return banks[:, kv_bank(p):kv_bank(p) + 2, :].rearrange("n i (g c) -> n (i g) c", g=CH)

        wkv_landed = sem("wkv_landed")
        wqo_landed = sem("wqo_landed")
        affine_landed = sem("affine_landed")
        x_landed = [sem(f"x_landed{i}") for i in range(6)]
        mask_step = sem("mask_step")
        consts_ready = sem("consts_ready")
        w_hi_ready = sem("w_hi_ready")
        w_lo_ready = sem("w_lo_ready")
        x_hi_ready = sem("x_hi_ready")
        x_lo_ready = sem("x_lo_ready")
        first_lo_ready = sem("first_lo_ready")
        kv_ready = sem("kv_ready")
        max_ready = sem("max_ready")
        shift_ready = sem("shift_ready")
        exp_ready = sem("exp_ready")
        sum_ready = sem("sum_ready")
        inv_ready = sem("inv_ready")
        probs_ready = sem("probs_ready")
        v_ready = sem("v_ready")
        ct_ready = sem("ct_ready")
        ct_masked = sem("ct_masked")
        u_ready = sem("u_ready")
        u_copied = sem("u_copied")
        a_ready = sem("a_ready")
        a_hi_ready = sem("a_hi_ready")
        a_lo_ready = sem("a_lo_ready")
        y_ready = sem("y_ready")
        y_copied = sem("y_copied")
        y_counted = sem("y_counted")
        aggregated = sem("aggregated")
        rstd_ready = sem("rstd_ready")
        mean_gamma_ready = sem("mean_gamma_ready")
        affine_ready = sem("affine_ready")
        std_ready = sem("std_ready")
        out_by_vector = sem("out_by_vector")
        out_by_scalar = sem("out_by_scalar")
        stored = sem("stored")

        PIECES = [(0, 1), (1, 2), (2, 4), (4, 6), (6, 8), (8, 16)]
        x_view = x_sb[:, :, :].rearrange("c p (b n) -> c (p b) n", n=N)
        y_view = y_sb[:, :, :].rearrange("c p (b n) -> c (p b) n", n=N)

        def parts(p, alone):
            return [(0, 1), (1, 2)] if p in alone else [(0, 2)]

        def run_slots(*stages):
            for t in range(-8, PAIRS + 8):
                for stage, back, alone, *some in stages:
                    first, end = some or (0, PAIRS)
                    if first <= t - back < end:
                        for lo, hi in parts(t - back, alone):
                            stage(t - back, lo, hi)

        SOFTMAX = (0, 1, LAST)
        CONTEXT = (LAST,)

        def ct_ps(p, lo, hi):
            return banks[:, 3 if (p, lo) == (LAST, 1) else 4, lo * T:hi * T]

        def u_ps(p, lo, hi):
            return banks[:, 1 if (p, lo) == (LAST, 1) else 5, lo * C:hi * C]

        def a_ps(p, lo, hi):
            return banks[:, 4 if (p, lo) == (LAST, 1) else 6, lo * C:hi * C]

        def y_ps(p, lo, hi):
            if p == LAST:
                return banks[:, lo, 0:N]
            return banks[:, 2 if p == IN_PSUM else 7, lo * N:hi * N]

        def y_source(lo, hi):
            if hi <= 2 * IN_PSUM:
                return y_view[:, lo:hi, :]
            if lo == 2 * LAST:
                return banks[:, 0:2, 0:N]
            return y_ps(lo // 2, 0, 2).rearrange("c (b n) -> c b n", n=N)

        block = ctx.enter_context(nc.Block())

        @block.sync
        def _(sp):
            for i, (lo, hi) in enumerate(PIECES):
                sp.dma_start(x_view[:, lo:hi, :], x[lo:hi].rearrange("b c n -> c b n")).then_inc(x_landed[i], 16)
                if i == 0:
                    sp.dma_start(w_sb[:, 0:2 * C], w[:, 0:2 * C]).then_inc(wkv_landed, 16)
                if i == 3:
                    sp.dma_start(w_sb[:, 2 * C:4 * C], w[:, 2 * C:4 * C]).then_inc(wqo_landed, 16)
            sp.dma_start(gamma_beta[:, :], affine).then_inc(affine_landed, 16)
            vector_steps = scalar_steps = 0
            for lo, hi, made_by in STORES:
                for engine, _, _ in made_by:
                    if engine == "vector":
                        vector_steps += 1
                        sp.wait_ge(out_by_vector, vector_steps)
                    else:
                        scalar_steps += 1
                        sp.wait_ge(out_by_scalar, scalar_steps)
                sp.dma_start(out[lo:hi].rearrange("b c n -> c b n"), y_view[:, lo:hi, :]).then_inc(stored, 16)
            sp.wait_ge(stored, 16 * len(STORES))

        @block.gpsimd
        def _(pool):
            nc.gpsimd.memset(same_head[:, :], 1.0).then_inc(mask_step, 1)
            nc.gpsimd.memset(identity[:, :, :], 0.0).then_inc(mask_step, 1)
            pool.wait_ge(mask_step, 2)
            blocks = same_head[:, :].rearrange("p (h d) -> p h d", d=D)
            nc.gpsimd.affine_select(out=blocks, in_=blocks, compare_op=ALU.is_ge, fill=0.0, base=0,
                                    pattern=[[-D, HEADS], [0, D]], channel_multiplier=1).then_inc(mask_step, 1)
            pool.wait_ge(mask_step, 3)
            nc.gpsimd.affine_select(out=blocks, in_=blocks, compare_op=ALU.is_ge, fill=0.0, base=D - 1,
                                    pattern=[[D, HEADS], [0, D]], channel_multiplier=-1).then_inc(mask_step, 1)
            pool.wait_ge(mask_step, 4)
            nc.gpsimd.tensor_tensor(head_mask[:, :], same_head[:, 0:T], same_head[:, T:2 * T],
                                    ALU.add).then_inc(consts_ready, 1)
            nc.gpsimd.affine_select(out=identity[:, :, :], in_=identity[:, :, :], compare_op=ALU.not_equal,
                                    fill=1.0, base=0, pattern=[[0, 2], [-1, C]],
                                    channel_multiplier=1).then_inc(consts_ready, 1)

            def split_lo(p, lo, hi):
                px = slice(lo * N, hi * N)
                pool.wait_ge(x_hi_ready, 2 * p + hi)
                nc.gpsimd.tensor_tensor(x_lo[:, p, px], x_sb[:, p, px], x_hi[:, p, px].bitcast(F32),
                                        ALU.subtract).then_inc(x_lo_ready, hi - lo)

            def normalise(p, lo, hi):
                pool.wait_ge(inv_ready, 2 * p + hi)
                inv = k_inv[:, p, lo:hi, :].rearrange("n i (g o) -> n (i g) o", o=1)
                heads = probs[:, p, CH * lo:CH * hi].rearrange("n g (h d) -> n (g h) d", d=D)
                nc.gpsimd.tensor_tensor(heads, heads, inv.to_broadcast([128, (hi - lo) * CH * HEADS, D]),
                                        ALU.mult).then_inc(probs_ready, hi - lo)

            run_slots((normalise, -2, SOFTMAX), (split_lo, -6, SOFTMAX, LO_BY_VECTOR, PAIRS))

        @block.scalar
        def _(act):
            def split_hi(p, lo, hi):
                for i, (first, end) in enumerate(PIECES):
                    if 2 * p + lo <= first < 2 * p + hi:
                        act.wait_ge(x_landed[i], 16)
                px = slice(lo * N, hi * N)
                nc.scalar.activation(x_hi[:, p, px], x_sb[:, p, px], ACT.Copy).then_inc(x_hi_ready, hi - lo)

            def exponentials(p, lo, hi):
                act.wait_ge(shift_ready, 2 * p + hi)
                chunks = probs[:, p, CH * lo:CH * hi]
                nc.scalar.activation(chunks, chunks, ACT.Exp).then_inc(exp_ready, hi - lo)

            def copy_values(p, lo, hi):
                act.wait_ge(shift_ready, 2 * p + hi)
                chunks = slice(CH * lo, CH * hi)
                nc.scalar.activation(v_sb[:, p, chunks], kv_ps(p)[:, chunks, C:2 * C],
                                     ACT.Copy).then_inc(v_ready, hi - lo)

            def copy_u(p, lo, hi):
                act.wait_ge(u_ready, 2 * p + hi)
                nc.scalar.activation(u_sb[:, p, lo * C:hi * C], u_ps(p, lo, hi), ACT.Copy).then_inc(u_copied, hi - lo)

            def split_a_hi(p, lo, hi):
                act.wait_ge(a_ready, 2 * p + hi)
                nc.scalar.activation(a_hi[:, p, lo * C:hi * C], a_ps(p, lo, hi), ACT.Copy
                                     ).then_inc(a_hi_ready, hi - lo)

            def copy_y(p, lo, hi):
                act.wait_ge(y_ready, 2 * p + hi)
                nc.scalar.activation(y_sb[:, p, :], y_ps(p, lo, hi), ACT.Copy).then_inc(y_copied, hi - lo)

            run_slots((exponentials, 0, SOFTMAX), (copy_values, 0, SOFTMAX), (split_hi, -4, SOFTMAX),
                      (split_a_hi, 3, CONTEXT), (copy_y, 4, CONTEXT, 0, IN_PSUM), (copy_u, 2, CONTEXT))
            act.wait_ge(aggregated, 1)
            nc.scalar.activation(std[:, :], mean_var[:, 1:2], ACT.Sqrt, bias=eps[:, 0:1]).then_inc(std_ready, 1)
            act.wait_ge(affine_ready, 2)
            for engine, lo, hi in (step for _, _, made_by in STORES for step in made_by):
                if engine == "scalar":
                    nc.scalar.activation(y_view[:, lo:hi, :], y_source(lo, hi), ACT.Identity,
                                         bias=shift[:, 0:1], scale=scale[:, 0:1]).then_inc(out_by_scalar, 1)

        @block.vector
        def _(dve):
            nc.vector.memset(eps[:, :], EPS)
            dve.wait_ge(wkv_landed, 16)
            nc.vector.tensor_copy(wkv_hi[:, :], wkv).then_inc(w_hi_ready, 1)
            dve.wait_ge(w_hi_ready, 1)
            nc.vector.tensor_tensor(wkv_lo[:, :], wkv, wkv_hi[:, :].bitcast(F32), ALU.subtract).then_inc(w_lo_ready, 1)

            def split_lo(p, lo, hi):
                dve.wait_ge(x_hi_ready, 2 * p + hi)
                px = slice(lo * N, hi * N)
                nc.vector.tensor_tensor(x_lo[:, p, px], x_sb[:, p, px], x_hi[:, p, px].bitcast(F32),
                                        ALU.subtract).then_inc(first_lo_ready, hi - lo)

            def keys(p, lo, hi):
                return kv_ps(p)[:, CH * lo:CH * hi, 0:C].rearrange("n g (h d) -> n g h d", d=D)

            def largest_keys(p, lo, hi):
                dve.wait_ge(kv_ready, 2 * p + hi)
                nc.vector.tensor_reduce(k_max[:, p, lo:hi, :], keys(p, lo, hi), AX.X, ALU.max
                                        ).then_inc(max_ready, hi - lo)

            def shift_keys(p, lo, hi):
                dve.wait_ge(max_ready, 2 * p + hi)
                largest = k_max[:, p, lo:hi, :].rearrange("n i (g h o) -> n (i g) h o", g=CH, o=1)
                nc.vector.tensor_tensor(probs[:, p, CH * lo:CH * hi].rearrange("n g (h d) -> n g h d", d=D),
                                        keys(p, lo, hi), largest.to_broadcast([128, (hi - lo) * CH, HEADS, D]),
                                        ALU.subtract).then_inc(shift_ready, hi - lo)

            def sum_heads(p, lo, hi):
                dve.wait_ge(exp_ready, 2 * p + hi)
                nc.vector.tensor_reduce(k_sum[:, p, lo:hi, :],
                                        probs[:, p, CH * lo:CH * hi].rearrange("n g (h d) -> n (g h) d", d=D),
                                        AX.X, ALU.add).then_inc(sum_ready, hi - lo)

            def invert_sums(p, lo, hi):
                dve.wait_ge(sum_ready, 2 * p + hi)
                nc.vector.reciprocal(k_inv[:, p, lo:hi, :], k_sum[:, p, lo:hi, :]).then_inc(inv_ready, hi - lo)

            def mask_context(p, lo, hi):
                dve.wait_ge(ct_ready, 2 * p + hi)
                if p == 0:
                    dve.wait_ge(consts_ready, 2)
                mask = head_mask[:, :].rearrange("e (o d) -> e o d", o=1).to_broadcast([C, hi - lo, T])
                nc.vector.tensor_tensor(ct_sb[:, p, lo:hi], ct_ps(p, lo, hi).rearrange("e (b d) -> e b d", b=hi - lo),
                                        mask, ALU.mult).then_inc(ct_masked, hi - lo)

            def split_a_lo(p, lo, hi):
                dve.wait_ge(a_hi_ready, 2 * p + hi)
                nc.vector.tensor_tensor(a_lo[:, p, lo * C:hi * C], a_ps(p, lo, hi),
                                        a_hi[:, p, lo * C:hi * C].bitcast(F32),
                                        ALU.subtract).then_inc(a_lo_ready, hi - lo)

            def count_y(p, lo, hi):
                if p < IN_PSUM:
                    dve.wait_ge(y_copied, 2 * p + hi)
                    y = y_sb[:, p, :]
                else:
                    dve.wait_ge(y_ready, 2 * p + hi)
                    y = y_ps(p, lo, hi)
                nc.vector.bn_stats(stats[:, (p + lo) * 6:(p + lo + 1) * 6], y).then_inc(y_counted, 1)

            run_slots((split_lo, -1, SOFTMAX, 0, LO_BY_VECTOR), (largest_keys, 0, SOFTMAX),
                      (mask_context, 3, CONTEXT), (shift_keys, 0, SOFTMAX, 0, 2),
                      (shift_keys, 0, SOFTMAX, 3, PAIRS), (sum_heads, 1, SOFTMAX), (split_a_lo, 4, CONTEXT),
                      (invert_sums, 1, SOFTMAX), (shift_keys, 0, SOFTMAX, 2, 3), (count_y, 5, CONTEXT))
            dve.wait_ge(y_counted, PAIRS + 1)
            nc.vector.bn_aggr(mean_var[:, :], stats[:, :]).then_inc(aggregated, 1)
            dve.wait_ge(aggregated, 1)
            dve.wait_ge(affine_landed, 16)
            nc.vector.tensor_tensor(mean_gamma[:, :], mean_var[:, 0:1], gamma_beta[:, 0:1],
                                    ALU.mult).then_inc(mean_gamma_ready, 1)
            dve.wait_ge(std_ready, 1)
            nc.vector.reciprocal(rstd[:, :], std[:, :]).then_inc(rstd_ready, 1)
            dve.wait_ge(rstd_ready, 1)
            nc.vector.tensor_tensor(scale[:, :], rstd[:, :], gamma_beta[:, 0:1], ALU.mult).then_inc(affine_ready, 1)
            dve.wait_ge(mean_gamma_ready, 1)
            nc.vector.scalar_tensor_tensor(out=shift[:, :], in0=mean_gamma[:, :], scalar=rstd[:, 0:1],
                                           in1=gamma_beta[:, 1:2], op0=ALU.mult, op1=ALU.subtract,
                                           reverse1=True).then_inc(affine_ready, 1)
            dve.wait_ge(affine_ready, 2)
            for engine, lo, hi in (step for _, _, made_by in STORES for step in made_by):
                if engine == "vector":
                    nc.vector.tensor_scalar(y_view[:, lo:hi, :], y_source(lo, hi), scale[:, 0:1], shift[:, 0:1],
                                            ALU.mult, ALU.add).then_inc(out_by_vector, 1)

        @block.tensor
        def _(pe):
            def project(p, lo, hi):
                if p == 0:
                    pe.wait_ge(w_hi_ready, 1)
                for image in range(lo, hi):
                    pe.wait_ge(x_hi_ready, 2 * p + hi)
                    q = kv_before(p)
                    if q is not None:
                        pe.wait_ge(v_ready, 2 * q + (image + 1 if q in SOFTMAX else 2))

                    def pass_over(xs, ws, start, stop):
                        for g in range(CH * image, CH * image + CH):
                            last = nc.tensor.matmul(kv_ps(p)[:, g, :], xs[:, p, g * 128:(g + 1) * 128], ws[:, :],
                                                    start=start and g == CH * image, stop=stop, skip_group_check=True)
                        return last

                    pass_over(x_hi, wkv_hi, True, False)
                    if p == 0:
                        pe.wait_ge(w_lo_ready, 1)
                    pass_over(x_hi, wkv_lo, False, False)
                    if p < LO_BY_VECTOR:
                        pe.wait_ge(first_lo_ready, 2 * p + hi)
                    else:
                        pe.wait_ge(x_lo_ready, 2 * (p - LO_BY_VECTOR) + hi)
                    pass_over(x_lo, wkv_hi, False, True).then_inc(kv_ready, 1)

            def context(p, lo, hi):
                pe.wait_ge(probs_ready, 2 * p + hi)
                pe.wait_ge(v_ready, 2 * p + hi)
                if p >= 1:
                    pe.wait_ge(ct_masked, 2 * p)
                for image in range(lo, hi):
                    ct = ct_ps(p, lo, hi)[:, (image - lo) * T:(image - lo + 1) * T]
                    for g in range(CH):
                        for t in range(0, C, T):
                            last = nc.tensor.matmul(ct[t:t + T, :], v_sb[:, p, image * CH + g, t:t + T],
                                                    probs[:, p, image * CH + g, t:t + T], start=(g == 0),
                                                    stop=(g == CH - 1), tile_position=(0, t), skip_group_check=True)
                last.then_inc(ct_ready, hi - lo)

            def times_wo(p, lo, hi):
                if p == 0:
                    pe.wait_ge(wqo_landed, 16)
                pe.wait_ge(ct_masked, 2 * p + hi)
                if p >= 1:
                    pe.wait_ge(u_copied, 2 * p)
                for image in range(lo, hi):
                    u = u_ps(p, lo, hi)[:, (image - lo) * C:(image - lo + 1) * C]
                    for t in range(0, C, T):
                        last = nc.tensor.matmul(u[t:t + T, :], ct_sb[t:t + T, p, image, :], woT[t:t + T, :],
                                                start=True, stop=True, tile_position=(t, t), skip_group_check=True)
                last.then_inc(u_ready, hi - lo)

            def times_wq(p, lo, hi):
                if p == 0:
                    pe.wait_ge(consts_ready, 2)
                    pe.wait_ge(v_ready, 2 * (EXTRA + 1))
                else:
                    pe.wait_ge(a_lo_ready, 2 * p)
                if (p, lo) == (LAST, 1):
                    pe.wait_ge(ct_masked, 2 * LAST + 1)
                nc.tensor.matmul(a_ps(p, lo, hi), identity[:, 0, :], identity[:, lo:hi, :].rearrange("c b o -> c (b o)"),
                                 start=True, stop=False)
                pe.wait_ge(u_copied, 2 * p + hi)
                nc.tensor.matmul(a_ps(p, lo, hi), wq, u_sb[:, p, lo * C:hi * C], start=False, stop=True
                                 ).then_inc(a_ready, hi - lo)

            def apply(p, lo, hi):
                pe.wait_ge(a_hi_ready, 2 * p + hi)
                if p in (IN_PSUM, LAST):
                    pe.wait_ge(v_ready, 2 * PAIRS)
                elif p >= 1:
                    pe.wait_ge(y_copied, 2 * min(p, IN_PSUM))

                def pass_over(a, xs, start, stop):
                    for image in range(lo, hi):
                        y = y_ps(p, image, image + 1)
                        last = nc.tensor.matmul(y, a[:, p, image * C:(image + 1) * C], xs[:, p, image * N:(image + 1) * N],
                                                start=start and image == lo, stop=stop, skip_group_check=True)
                    return last

                pass_over(a_hi, x_hi, True, False)
                pass_over(a_hi, x_lo, False, False)
                pe.wait_ge(a_lo_ready, 2 * p + hi)
                last = pass_over(a_lo, x_hi, False, True)
                last.then_inc(y_ready, hi - lo)

            zeros = nc.const_aps.tensor(0.0, [128, 128], F32)
            for _ in range(WARM_UP):
                nc.tensor.matmul(banks[:, 7, 0:128], zeros, zeros, start=True, stop=True)

            run_slots((project, 0, SOFTMAX), (times_wo, 4, CONTEXT, 0, 1), (context, 3, CONTEXT),
                      (times_wq, 4, CONTEXT), (apply, 5, CONTEXT), (times_wo, 3, CONTEXT, 1, PAIRS))


def kernel(x, L0_conv_Wq, L0_conv_Wk, L0_conv_Wv, L0_conv_Wo, L0_conv_gamma, L0_conv_beta):
    import numpy as np
    import concourse.bacc as bacc
    from concourse.bass_utils import run_bass_kernel_spmd

    x = np.asarray(x)
    shape = x.shape
    arrays = {
        "x_dram": np.ascontiguousarray(x).reshape(B, C, N),
        "w_dram": np.concatenate([np.asarray(L0_conv_Wk).T, np.asarray(L0_conv_Wv).T,
                                  np.asarray(L0_conv_Wq), np.asarray(L0_conv_Wo).T], axis=1),
        "affine_dram": np.stack([np.asarray(L0_conv_gamma), np.asarray(L0_conv_beta)], axis=1),
    }
    nc = bacc.Bacc("TRN2", target_bir_lowering=False, num_devices=1)
    args = [nc.dram_tensor(n, a.shape, mybir.dt.from_np(a.dtype), kind="ExternalInput").ap()
            for n, a in arrays.items()]
    args.append(nc.dram_tensor("out_dram", (B, C, N), F32, kind="ExternalOutput").ap())
    attention_batchnorm(nc, *args)
    result = run_bass_kernel_spmd(nc, [arrays], core_ids=[0])
    return result.results[0]["out_dram"].reshape(shape)
```
